# Optimizing a Trainium2 kernel written in Bass

```python
import numpy as np
import jax
import jax.numpy as jnp

def _softmax(x, axis=-1):
    return jax.nn.softmax(x, axis=axis)

def _gelu(x):
    return jax.nn.gelu(x, approximate=True)

def _silu(x):
    return jax.nn.silu(x)

def _sigmoid(x):
    return jax.nn.sigmoid(x)

def _layernorm(x, axis=-1, eps=1e-05):
    m = jnp.mean(x, axis=axis, keepdims=True)
    v = jnp.var(x, axis=axis, keepdims=True)
    return (x - m) / jnp.sqrt(v + eps)

def _scatter_add(tgt, idx, src, axis=0):
    return tgt.at[idx].add(src)

def _segment_sum(src, seg, n):
    return jax.ops.segment_sum(src, seg, n)
kernel_name = 'mk_gnn_preln_d4_gnn_r64_570b59'

def setup_inputs(seed: int=0):
    np.random.seed(seed)
    _w = jnp.asarray

    def _rec_inputs():
        import jax
        import jax.numpy as jnp
        _gk = jax.random.key(seed)
        x = -0.000202 + 1 * jax.random.normal(jax.random.fold_in(_gk, 1), (100000, 64), jnp.float32)
        src = jax.random.randint(jax.random.fold_in(_gk, 2), (25000,), 0, 100000, jnp.int32)
        dst = jax.random.randint(jax.random.fold_in(_gk, 3), (25000,), 0, 100000, jnp.int32)
        _o = jnp.argsort(dst, stable=True)
        src = src[_o]
        dst = dst[_o]
        edge_attr_32 = -9.77346e-05 + 0.999888 * jax.random.normal(jax.random.fold_in(_gk, 12), (25000, 32), jnp.float32)
        return (x, src, dst, edge_attr_32)
    x, src, dst, edge_attr_32 = _rec_inputs()

    def _L0_gnn_setup():
        import jax, jax.numpy as jnp
        import numpy as np
        N_NODES = 100000
        N_EDGES = 25000
        N_FEAT = 64
        E_FEAT = 32
        OUT_FEAT = 64

        def _xavier_normal(key, shape, gain):
            fan_out, fan_in = shape
            std = gain * np.sqrt(2.0 / (fan_in + fan_out))
            return jax.random.normal(key, shape, dtype=jnp.float32) * std
        key = jax.random.key(seed)
        ks = jax.random.split(key, 9)
        d_cat = 2 * N_FEAT + E_FEAT
        n_feat = jax.random.normal(ks[0], (N_NODES, N_FEAT), dtype=jnp.float32)
        e_feat = jax.random.normal(ks[1], (N_EDGES, E_FEAT), dtype=jnp.float32)
        src = jax.random.randint(ks[2], (N_EDGES,), 0, N_NODES, dtype=jnp.int32)
        dst = jax.random.randint(ks[3], (N_EDGES,), 0, N_NODES, dtype=jnp.int32)
        gain = np.sqrt(2.0)
        bound_msg = 1.0 / np.sqrt(d_cat)
        return {'n_feat': n_feat, 'e_feat': e_feat, 'src': src, 'dst': dst, 'W_msg_w': jax.random.uniform(ks[4], (OUT_FEAT, d_cat), jnp.float32, -bound_msg, bound_msg), 'W_msg_b': jax.random.uniform(ks[5], (OUT_FEAT,), jnp.float32, -bound_msg, bound_msg), 'W_w': _xavier_normal(ks[6], (2 * OUT_FEAT, d_cat), gain), 'W_b': jax.random.uniform(ks[7], (2 * OUT_FEAT,), jnp.float32, -bound_msg, bound_msg), 'a': _xavier_normal(ks[8], (2 * OUT_FEAT, 1), gain)}
    _L0_gnn_all = _L0_gnn_setup()
    _L0_gnn_in = {k: v for k, v in _L0_gnn_all.items() if k in ('W_msg_w', 'W_msg_b', 'W_w', 'W_b', 'a')}
    del _L0_gnn_all

    def _L1_gnn_setup():
        import jax, jax.numpy as jnp
        import numpy as np
        N_NODES = 100000
        N_EDGES = 25000
        D = 64
        key = jax.random.key(seed)
        k1, k2, k3, k4 = jax.random.split(key, 4)
        feat = jax.random.normal(k1, (N_NODES, D), dtype=jnp.float32)
        src = jax.random.randint(k2, (N_EDGES,), 0, N_NODES, dtype=jnp.int32)
        dst = jax.random.randint(k3, (N_EDGES,), 0, N_NODES, dtype=jnp.int32)
        bound = 1.0 / np.sqrt(D)
        fc_w = jax.random.uniform(k4, (D, D), dtype=jnp.float32, minval=-bound, maxval=bound)
        fc_b = jnp.zeros((D,), dtype=jnp.float32)
        return {'feat': feat, 'src': src, 'dst': dst, 'fc_w': fc_w, 'fc_b': fc_b}
    _L1_gnn_all = _L1_gnn_setup()
    _L1_gnn_in = {k: v for k, v in _L1_gnn_all.items() if k in ('fc_w', 'fc_b')}
    del _L1_gnn_all

    def _L2_gnn_setup():
        import jax, jax.numpy as jnp
        import numpy as np
        N_NODES = 50000
        N_EDGES = 12500
        D = 64

        def gcn_conv(x, W, b, src, dst, norm, num_nodes):
            h = x @ W
            msg = h[src] * norm[:, None]
            out = jax.ops.segment_sum(msg, dst, num_segments=num_nodes)
            return out + b
        key = jax.random.key(seed)
        k1, k2, k3, k4 = jax.random.split(key, 4)
        x = jax.random.normal(k1, (N_NODES, D), dtype=jnp.float32)
        edge_index = jax.random.randint(k2, (2, N_EDGES), 0, N_NODES, dtype=jnp.int64)
        W1 = jax.random.normal(k3, (D, D), dtype=jnp.float32) / np.sqrt(D)
        b1 = jnp.zeros((D,), dtype=jnp.float32)
        W2 = jax.random.normal(k4, (D, D), dtype=jnp.float32) / np.sqrt(D)
        b2 = jnp.zeros((D,), dtype=jnp.float32)
        return {'x': x, 'edge_index': edge_index, 'W1': W1, 'b1': b1, 'W2': W2, 'b2': b2}
    _L2_gnn_all = _L2_gnn_setup()
    _L2_gnn_in = {k: v for k, v in _L2_gnn_all.items() if k in ('W1', 'b1', 'W2', 'b2')}
    del _L2_gnn_all

    def _L3_gnn_setup():
        import jax, jax.numpy as jnp
        import numpy as np
        N_NODES = 100000

        def gcn_conv(x, src, dst, W, b):
            n = x.shape[0]
            xw = x @ W
            deg = jax.ops.segment_sum(jnp.ones_like(dst, dtype=xw.dtype), dst, num_segments=n)
            dinv = jnp.where(deg > 0, jax.lax.rsqrt(deg), 0.0)
            norm = dinv[src] * dinv[dst]
            out = jax.ops.segment_sum(norm[:, None] * xw[src], dst, num_segments=n)
            return out + b
        key = jax.random.key(seed)
        k1, k2, k3, k4, k5, k6 = jax.random.split(key, 6)
        d = 64
        E = 25000
        x = jax.random.normal(k1, (N_NODES, d), dtype=jnp.float32)
        edge_index = jax.random.randint(k2, (2, E), 0, N_NODES, dtype=jnp.int64)
        s = 1.0 / np.sqrt(d)
        W1 = jax.random.normal(k3, (d, d), dtype=jnp.float32) * s
        b1 = jax.random.normal(k4, (d,), dtype=jnp.float32) * 0.01
        W2 = jax.random.normal(k5, (d, d), dtype=jnp.float32) * s
        b2 = jax.random.normal(k6, (d,), dtype=jnp.float32) * 0.01
        return {'x': x, 'edge_index': edge_index, 'W1': W1, 'b1': b1, 'W2': W2, 'b2': b2}
    _L3_gnn_all = _L3_gnn_setup()
    _L3_gnn_in = {k: v for k, v in _L3_gnn_all.items() if k in ('W1', 'b1', 'W2', 'b2')}
    del _L3_gnn_all
    return {'x': x, 'src': src, 'dst': dst, 'edge_attr_32': edge_attr_32, 'L0_gnn_W_msg_w': _L0_gnn_in['W_msg_w'], 'L0_gnn_W_msg_b': _L0_gnn_in['W_msg_b'], 'L0_gnn_W_w': _L0_gnn_in['W_w'], 'L0_gnn_W_b': _L0_gnn_in['W_b'], 'L0_gnn_a': _L0_gnn_in['a'], 'L1_gnn_fc_w': _L1_gnn_in['fc_w'], 'L1_gnn_fc_b': _L1_gnn_in['fc_b'], 'L2_gnn_W1': _L2_gnn_in['W1'], 'L2_gnn_b1': _L2_gnn_in['b1'], 'L2_gnn_W2': _L2_gnn_in['W2'], 'L2_gnn_b2': _L2_gnn_in['b2'], 'L3_gnn_W1': _L3_gnn_in['W1'], 'L3_gnn_b1': _L3_gnn_in['b1'], 'L3_gnn_W2': _L3_gnn_in['W2'], 'L3_gnn_b2': _L3_gnn_in['b2']}

def reference(x, src, dst, edge_attr_32, L0_gnn_W_msg_w, L0_gnn_W_msg_b, L0_gnn_W_w, L0_gnn_W_b, L0_gnn_a, L1_gnn_fc_w, L1_gnn_fc_b, L2_gnn_W1, L2_gnn_b1, L2_gnn_W2, L2_gnn_b2, L3_gnn_W1, L3_gnn_b1, L3_gnn_W2, L3_gnn_b2):
    import jax
    import jax.numpy as jnp

    def _L0_gnn_ref(n_feat, e_feat, src, dst, W_msg_w, W_msg_b, W_w, W_b, a):
        import jax, jax.numpy as jnp
        import numpy as np
        N_NODES = 100000
        N_EDGES = 25000
        N_FEAT = 64
        E_FEAT = 32
        OUT_FEAT = 64

        def _xavier_normal(key, shape, gain):
            fan_out, fan_in = shape
            std = gain * np.sqrt(2.0 / (fan_in + fan_out))
            return jax.random.normal(key, shape, dtype=jnp.float32) * std
        feat_cat = jnp.concatenate([n_feat[src], n_feat[dst], e_feat], axis=1)
        w_feat = feat_cat @ W_w.T + W_b
        logits = jax.nn.leaky_relu(w_feat @ a[:, 0])
        seg_max = jax.ops.segment_max(logits, dst, num_segments=N_NODES)
        ex = jnp.exp(logits - seg_max[dst])
        seg_sum = jax.ops.segment_sum(ex, dst, num_segments=N_NODES)
        att = ex / seg_sum[dst]
        msg = feat_cat @ W_msg_w.T + W_msg_b
        agg = jax.ops.segment_sum(att[:, None] * msg, dst, num_segments=N_NODES)
        return jax.nn.relu(agg)

    def _L1_gnn_ref(feat, src, dst, fc_w, fc_b):
        import jax, jax.numpy as jnp
        import numpy as np
        N_NODES = 100000
        N_EDGES = 25000
        D = 64
        ones = jnp.ones((src.shape[0],), dtype=jnp.float32)
        out_deg = jnp.clip(jax.ops.segment_sum(ones, src, num_segments=N_NODES), 1.0)
        in_deg = jnp.clip(jax.ops.segment_sum(ones, dst, num_segments=N_NODES), 1.0)
        h = feat @ fc_w.T + fc_b
        h = h * (out_deg ** (-0.5))[:, None]
        agg = jax.ops.segment_sum(h[src], dst, num_segments=N_NODES)
        rst = agg * (in_deg ** (-0.5))[:, None]
        rst = rst + feat
        return rst

    def _L2_gnn_ref(x, edge_index, W1, b1, W2, b2):
        import jax, jax.numpy as jnp
        import numpy as np
        N_NODES = 50000
        N_EDGES = 12500
        D = 64

        def gcn_conv(x, W, b, src, dst, norm, num_nodes):
            h = x @ W
            msg = h[src] * norm[:, None]
            out = jax.ops.segment_sum(msg, dst, num_segments=num_nodes)
            return out + b
        num_nodes = x.shape[0]
        loops = jnp.arange(num_nodes, dtype=edge_index.dtype)
        src = jnp.concatenate([edge_index[0], loops])
        dst = jnp.concatenate([edge_index[1], loops])
        deg = jax.ops.segment_sum(jnp.ones_like(dst, dtype=x.dtype), dst, num_segments=num_nodes)
        dis = jnp.where(deg > 0, jax.lax.rsqrt(jnp.maximum(deg, 1.0)), 0.0)
        norm = dis[src] * dis[dst]
        out = gcn_conv(x, W1, b1, src, dst, norm, num_nodes)
        out = jax.nn.relu(out)
        out = jnp.where(out >= 0, out, 0.1 * out)
        out = gcn_conv(out, W2, b2, src, dst, norm, num_nodes)
        out = out + x
        return out

    def _L3_gnn_ref(x, edge_index, W1, b1, W2, b2):
        import jax, jax.numpy as jnp
        import numpy as np
        N_NODES = 100000

        def gcn_conv(x, src, dst, W, b):
            n = x.shape[0]
            xw = x @ W
            deg = jax.ops.segment_sum(jnp.ones_like(dst, dtype=xw.dtype), dst, num_segments=n)
            dinv = jnp.where(deg > 0, jax.lax.rsqrt(deg), 0.0)
            norm = dinv[src] * dinv[dst]
            out = jax.ops.segment_sum(norm[:, None] * xw[src], dst, num_segments=n)
            return out + b
        n = x.shape[0]
        loops = jnp.arange(n, dtype=edge_index.dtype)
        src = jnp.concatenate([edge_index[0], loops])
        dst = jnp.concatenate([edge_index[1], loops])
        out = jax.nn.relu(gcn_conv(x, src, dst, W1, b1))
        out = gcn_conv(out, src, dst, W2, b2)
        return jax.nn.relu(out + x)
    edge_index = jnp.stack([src, dst])
    h = jnp.maximum(_layernorm(x, axis=-1), 0.0)
    x = x + _L0_gnn_ref(h, edge_attr_32, src, dst, L0_gnn_W_msg_w, L0_gnn_W_msg_b, L0_gnn_W_w, L0_gnn_W_b, L0_gnn_a)
    h = jnp.maximum(_layernorm(x, axis=-1), 0.0)
    x = x + _L1_gnn_ref(h, src, dst, L1_gnn_fc_w, L1_gnn_fc_b)
    h = jnp.maximum(_layernorm(x, axis=-1), 0.0)
    x = x + _L2_gnn_ref(h, edge_index, L2_gnn_W1, L2_gnn_b1, L2_gnn_W2, L2_gnn_b2)
    h = jnp.maximum(_layernorm(x, axis=-1), 0.0)
    x = x + _L3_gnn_ref(h, edge_index, L3_gnn_W1, L3_gnn_b1, L3_gnn_W2, L3_gnn_b2)
    return x

_drawn_inputs = setup_inputs


def setup_inputs(seed=0):
    import zlib

    import numpy as np

    out = dict(_drawn_inputs(seed))
    spreads = {'L1_gnn_fc_b': (0.0, 0.348), 'L2_gnn_b1': (0.0, 0.32), 'L2_gnn_b2': (0.0, 0.1)}
    factors = {'L0_gnn_W_msg_b': 3.227,
     'L0_gnn_W_w': 39.896,
     'L0_gnn_W_b': 200.0,
     'L0_gnn_a': 3.972,
     'L3_gnn_b1': 23.899,
     'L3_gnn_b2': 21.596}
    for name, (base, spread) in spreads.items():
        noise = np.random.default_rng([zlib.crc32(name.encode()), seed]).standard_normal(out[name].shape)
        drawn = base * np.exp(spread * noise) if base else spread * noise
        out[name] = jnp.asarray(drawn.astype(out[name].dtype))
    for name, factor in factors.items():
        out[name] = (out[name] * factor).astype(out[name].dtype)
    return out
```

```python
from contextlib import ExitStack

import concourse.bass as bass
from concourse import mybir
from concourse.alu_op_type import AluOpType as ALU

F32 = mybir.dt.float32
F16 = mybir.dt.float16
I32 = mybir.dt.int32
ACT = mybir.ActivationFunctionType

P = 128
N = 100000
E = 25000
F = 64
EF = 32
TILES = -(-E // P)
EPAD = TILES * P
GT = 4
GROUPS = TILES // GT
W = GT * P
UR = 2 * W
NODE_UNITS = -(-N // UR)
EDGE_UNITS = -(-EPAD // UR)
HALF = TILES // 2
LO = 512
HI = TILES
EPS = 1e-5
FAR = 1e30
ZERO_ROW = EPAD
UNROLL = 4




class Step:

    def __init__(self, h, off):
        self.h, self.off = h, off

    def at(self, c=0):
        return self.h * UNROLL + (self.off + c)

    def back(self, lag):
        return Step(self.h, self.off - lag)

    def ring(self, r):
        return self.off % r

    def turn(self, r):
        return self.h * (UNROLL // r) + self.off // r


def need(eng, sem, value, cap=None):
    if isinstance(value, int):
        if value <= 0:
            return
        if cap is not None:
            value = min(value, cap)
    eng.wait_ge(sem, value)


def pool_need(eng, s, sem, value):
    if isinstance(value, int) and value <= 0:
        return
    eng.wait_ge(sem, value)
    eng.sem_inc(s["passed"], 1)


def pipeline(eng, n, parts):
    most = max(lag for lag, _ in parts)

    def slot(h, off, check):
        for lag, fn in parts:
            if not check or 0 <= off - lag < n:
                fn(Step(h, off - lag))

    head = -(-(most + UNROLL + 1) // UNROLL) * UNROLL
    tail = n // UNROLL * UNROLL
    for t in range(head):
        slot(0, t, True)
    with eng.Fori(head // UNROLL, tail // UNROLL) as h:
        for j in range(UNROLL):
            slot(h, j, False)
    for t in range(tail, n + most):
        slot(0, t, True)


def build(nc, A, out):
    with ExitStack() as top:
        def sb(name, shape, dt=F32, ctx=top):
            return ctx.enter_context(nc.sbuf_tensor(name, shape, dt))

        def dram(name, shape, dt=F32):
            return nc.dram_tensor(name, shape, dt).ap()

        bank = [top.enter_context(nc.psum_tensor(f"bank{i}", [P, 512], F32)) for i in range(8)]
        C = dict(
            ident=sb("ident", [P, P]), center=sb("center", [P, P]), mean=sb("mean", [P, P]),
            eps=sb("eps", [P, 1]), wconv=sb("wconv", [P, 4, P]), bias=sb("bias", [P, 8]),
            fc=sb("fc", [F + 1, F]), wm_se=sb("wm_se", [96, F]), wm_d=sb("wm_d", [F, F]),
            v_se=sb("v_se", [96, P]), v_d=sb("v_d", [F, P]), c0=sb("c0", [P, 1]),
            take_sum=sb("take_sum", [P, F]),
            src=sb("src_i", [P, TILES], I32), dst=sb("dst_i", [P, TILES], I32),
            scat=sb("scat_i", [P, TILES], I32), slot=sb("slot_i", [P, TILES], I32),
            slotf=sb("slot_f", [P, TILES]), oscale=sb("oscale", [P, TILES]))
        D = dict(
            xs=dram("xs_rows", (EPAD, F)), xd=dram("xd_rows", (EPAD, F)),
            table=dram("node_table", (HI * LO, 2)),
            same=dram("same_row", (1, EPAD)), f2=dram("f2_row", (1, EPAD)),
            osc=dram("osc_row", (1, EPAD)),
            row_sets=[dram(f"row_set{i}", (1, 3, EPAD)) for i in range(2)],
            src_pairs=[dram(f"src_pairs{i}", (TILES // 2, P, P)) for i in range(5)],
            dst_pairs=[dram(f"dst_pairs{i}", (TILES // 2, P, P)) for i in range(2)],
            rows=[dram(f"slot_rows{i}", (EPAD + 1, F)) for i in range(5)],
            res=[dram(f"res{i}", (F, EPAD)) for i in range(3)],
            own=[dram(f"self{i}", (F, EPAD)) for i in range(4)],
            h3=dram("h3_cols", (F, EPAD)))
        K = dict(nc=nc, A=A, out=out, bank=bank, C=C, D=D, sb=sb)
        with ExitStack() as ctx:
            hist = index_phase(K, ctx)
            table_phase(K, ctx, hist)
        unit_phase(K, "node")
        mask_phase(K)
        unit_phase(K, "src")
        unit_phase(K, "dst")
        attention_phase(K)
        for stage in "BCDEF":
            edge_phase(K, stage)


def sems(nc, ctx, prefix, names):
    def made(name, keys):
        return {k: one(f"{prefix}_{name}{k}", ctx, nc) for k in keys}
    out = {}
    for name, _, ring in (n.partition(":") for n in names.split()):
        if ring == "n":
            out[name] = made(name, (1, 2, 3))
        elif ring:
            out[name] = made(name, range(int(ring)))
        else:
            out[name] = one(f"{prefix}_{name}", ctx, nc)
    return out


def one(name, ctx, nc):
    sem = nc.alloc_semaphore(name)
    ctx.phase_sems.append(sem)
    return sem


class Phase:

    def __init__(self, nc):
        self.nc, self.buffers, self.phase_sems = nc, ExitStack(), []

    def enter_context(self, buffer):
        return self.buffers.enter_context(buffer)

    def __enter__(self):
        return self

    def __exit__(self, kind, error, trace):
        if kind is None:
            self.nc.clear_and_free_semaphores(self.phase_sems)
            self.nc.all_engine_barrier()
        self.buffers.close()


def index_phase(K, outer):
    nc, A, C, D, bank = K["nc"], K["A"], K["C"], K["D"], K["bank"]
    H = dict(
        io=K["sb"]("iota_f16", [P, LO], F16, outer),
        shi=K["sb"]("shi", [P, TILES], F32, outer), slo=K["sb"]("slo", [P, TILES], F32, outer),
        dhi=K["sb"]("dhi", [P, TILES], F32, outer), dlo=K["sb"]("dlo", [P, TILES], F32, outer),
        w1=K["sb"]("w1", [P, TILES], F32, outer), w2=K["sb"]("w2", [P, TILES], F32, outer))
    with Phase(nc) as ctx:
        def sb(name, shape, dt=F32):
            return ctx.enter_context(nc.sbuf_tensor(name, shape, dt))
        ed = sb("ed_i", [HALF, 4, 256], I32)
        ef = sb("ed_f", [HALF, 4, 256])
        q = sb("q_f", [HALF, 8, 256])
        io = sb("io_i", [P, LO], I32)
        tn = sb("tn_i", [P, TILES], I32)
        pn = sb("pn_i", [P, 1], I32)
        tnf = sb("tn_f", [P, TILES])
        pnf = sb("pn_f", [P, 1])
        hl = sb("hl_i", [P, 2, TILES], I32)
        tf = sb("tf", [P, 4, TILES])
        ones = sb("ones", [P, 256])
        open_row = sb("open_row", [1, 128])
        carry = sb("carry", [1, 128])
        carry_col = sb("carry_col", [HALF, 1])
        zrow = sb("zrow", [1, F])
        wm = sb("wm", [F, 160])
        ww = sb("ww", [P, 160])
        wb = sb("wb", [P, 1])
        a_col = sb("a_col", [P, 1])
        a_rep = sb("a_rep", [P, P])
        fcw = sb("fcw", [F, F])
        s = sems(nc, ctx, "ix", "cleared loaded weights pool v pe evac rows")
        mark = {}
        with nc.Block() as block:
            NW = 9 + 8 + 10

            @block.vector
            def _(v):
                n = [0]

                def link(ins):
                    n[0] += 1
                    ins.then_inc(s["v"], 1)
                    v.wait_ge(s["v"], n[0])

                v.memset(ed[:, 0:2, :], N)
                v.memset(ed[:, 2:4, :], -1)
                v.memset(C["wconv"][:, :, :], 0.0)
                v.memset(zrow[:, :], 0.0).then_inc(s["cleared"], 1)
                link(v.memset(C["eps"][:, :], EPS))
                link(v.memset(ones[:, :], 1.0))
                link(v.memset(C["center"][:, :], 0.0))
                link(v.memset(C["mean"][:, :], 0.0))
                link(v.memset(C["take_sum"][:, :], 0.0))
                for i in range(2):
                    link(v.memset(C["center"][i * F:i * F + F, i * F:i * F + F], -1.0 / F))
                    link(v.memset(C["mean"][i * F:i * F + F, i * F:i * F + F], 1.0 / F))
                link(v.memset(C["take_sum"][96:P, :], 1.0 / 32))
                v.wait_ge(s["pool"], 5)
                link(v.tensor_tensor(C["center"][:, :], C["center"][:, :], C["ident"][:, :], ALU.add))
                link(v.tensor_copy(H["io"][:, :], io[:, :]))
                link(v.tensor_copy(tnf[:, :], tn[:, :]))
                link(v.tensor_copy(pnf[:, :], pn[:, :]))
                v.wait_ge(s["weights"], NW * 16)
                link(v.tensor_scalar(a_rep[:, :], ones[:, 0:P], a_col[:, 0:1], None, ALU.mult))
                mark["a"] = n[0]
                v.wait_ge(s["loaded"], 9 * 16)
                link(v.tensor_copy(ef[:, :, :], ed[:, :, :]))
                same, last = q[:, 0, :], q[:, 1, :]
                link(v.tensor_tensor(same, ef[:, 1, :], ef[:, 2, :], ALU.is_equal))
                link(v.tensor_tensor(last, ef[:, 1, :], ef[:, 3, :], ALU.not_equal))
                link(v.tensor_scalar(q[:, 2, :], last, -2.0 * N, 2.0 * N, ALU.mult, ALU.add))
                link(v.tensor_tensor(q[:, 2, :], q[:, 2, :], ef[:, 1, :], ALU.add))
                mark["q"] = n[0]
                link(v.tensor_tensor_scan(q[:, 3, :], same, ones[0:HALF, :], 0.0, ALU.mult, ALU.add))
                link(v.tensor_tensor_scan(q[:, 4, :], same, ones[0:HALF, :], 1.0, ALU.mult, ALU.mult))
                mark["scan"] = n[0]
                v.wait_ge(s["pe"], 1)
                link(v.memset(carry[:, :], 0.0))
                link(v.tensor_copy(open_row[:, 0:HALF], bank[0][0:1, 0:HALF]))
                link(v.tensor_tensor_scan(carry[0:1, 1:1 + HALF], open_row[:, 0:HALF],
                                          bank[0][0:1, 128:128 + HALF], 0.0, ALU.mult, ALU.add))
                mark["carry"] = n[0]
                v.wait_ge(s["pe"], 2)
                link(v.tensor_copy(carry_col[:, :], bank[1][0:HALF, 0:1]))
                link(v.scalar_tensor_tensor(q[:, 5, :], q[:, 4, :], carry_col[:, 0:1], q[:, 3, :],
                                            ALU.mult, ALU.add))
                link(v.tensor_scalar(q[:, 6, :], q[:, 5, :], 1.0, None, ALU.add))
                mark["count"] = n[0]
                v.wait_ge(s["evac"], 1)
                link(v.reciprocal(q[:, 5:7, :], q[:, 5:7, :]))
                mark["f"] = n[0]
                v.wait_ge(s["pe"], 3)
                for i in range(3):
                    for j in range(2):
                        link(v.tensor_copy(tf[:, i, j::2], bank[2 + i][:, 128 * j:128 * j + HALF]))
                link(v.tensor_copy(tf[:, 3, 0::2], bank[5][:, 0:HALF]))
                link(v.tensor_copy(tf[:, 3, 1::2], bank[5][:, 128:128 + HALF]))
                for i, (hi, lo, clipped) in enumerate(((H["shi"], H["slo"], C["src"]), (H["dhi"], H["dlo"], C["dst"]))):
                    link(v.tensor_copy(hl[:, 0, :], tf[:, i, :]))
                    link(v.tensor_scalar(hl[:, 1, :], hl[:, 0, :], 9, None, ALU.logical_shift_right))
                    link(v.tensor_copy(hi[:, :], hl[:, 1, :]))
                    link(v.tensor_scalar(hl[:, 1, :], hl[:, 0, :], LO - 1, None, ALU.bitwise_and))
                    link(v.tensor_copy(lo[:, :], hl[:, 1, :]))
                    link(v.tensor_scalar(clipped[:, :], tf[:, i, :], float(N - 1), None, ALU.min))
                link(v.tensor_copy(C["scat"][:, :], tf[:, 2, :]))
                link(v.tensor_tensor(H["w1"][:, :], tf[:, 3, :], tnf[:, :], ALU.mult))
                link(v.tensor_scalar(H["w2"][:, :], tf[:, 3, :], pnf[:, 0:1], None, ALU.mult))
                v.wait_ge(s["pe"], 4)
                link(v.tensor_copy(C["wm_se"][:, :], bank[6][0:96, 0:F]))
                link(v.tensor_copy(C["wm_d"][:, :], bank[6][0:F, 64:128]))
                link(v.tensor_copy(C["fc"][0:F, :], bank[6][0:F, 128:192]))
                link(v.tensor_copy(C["v_se"][:, :], bank[6][0:96, 256:384]))
                link(v.tensor_copy(C["v_d"][:, :], bank[6][0:F, 384:512]))
                link(v.tensor_copy(C["c0"][:, :], bank[7][:, 0:1]))

            @block.gpsimd
            def _(g):
                g.memset(C["ident"][:, :], 0.0).then_inc(s["pool"], 1)
                g.wait_ge(s["pool"], 1)
                g.affine_select(out=C["ident"][:, :], in_=C["ident"][:, :], compare_op=ALU.not_equal, fill=1.0,
                                base=0, pattern=[[-1, P]], channel_multiplier=1).then_inc(s["pool"], 1)
                g.iota(io[:, :], pattern=[[1, LO]], base=0, channel_multiplier=0).then_inc(s["pool"], 1)
                g.iota(tn[:, :], pattern=[[P, TILES]], base=P, channel_multiplier=0).then_inc(s["pool"], 1)
                g.iota(pn[:, :], pattern=[[0, 1]], base=0, channel_multiplier=1).then_inc(s["pool"], 1)

            @block.sync
            def _(sp):
                def load(dst_ap, src_ap, sem=s["weights"]):
                    sp.dma_start(dst_ap, src_ap).then_inc(sem, 16)

                sp.wait_ge(s["cleared"], 1)
                full = (HALF - 1) * 256
                rest = E - full
                for i, name in enumerate(("src", "dst")):
                    load(ed[0:HALF - 1, i, :], A[name][0:full].rearrange("(p c) -> p c", c=256), s["loaded"])
                    load(ed[HALF - 1:HALF, i, 0:rest], A[name][full:E].rearrange("(p c) -> p c", p=1), s["loaded"])
                dst = A["dst"]
                load(ed[0:1, 2, 1:256], dst[0:255].rearrange("(p c) -> p c", p=1), s["loaded"])
                load(ed[1:HALF - 1, 2, :], dst[255:full - 1].rearrange("(p c) -> p c", c=256), s["loaded"])
                load(ed[HALF - 1:HALF, 2, 0:rest + 1], dst[full - 1:E].rearrange("(p c) -> p c", p=1), s["loaded"])
                load(ed[0:HALF - 1, 3, :], dst[1:full + 1].rearrange("(p c) -> p c", c=256), s["loaded"])
                load(ed[HALF - 1:HALF, 3, 0:rest - 1], dst[full + 1:E].rearrange("(p c) -> p c", p=1), s["loaded"])
                wc = ("L2_gnn_W1", "L2_gnn_W2", "L3_gnn_W1", "L3_gnn_W2")
                for i, name in enumerate(wc):
                    for h in range(2):
                        load(C["wconv"][h * F:h * F + F, i, h * F:h * F + F], A[name])
                bc = ("L2_gnn_b1", "L2_gnn_b2", "L3_gnn_b1", "L3_gnn_b2", "L0_gnn_W_msg_b")
                for i, name in enumerate(bc):
                    for h in range(2):
                        load(C["bias"][h * F:h * F + F, i:i + 1], A[name].rearrange("(f o) -> f o", o=1))
                for tile_, name in ((wm, "L0_gnn_W_msg_w"), (ww, "L0_gnn_W_w")):
                    load(tile_[:, 0:F], A[name][:, 0:F])
                    load(tile_[:, F:96], A[name][:, 2 * F:160])
                    load(tile_[:, 96:160], A[name][:, F:2 * F])
                load(wb[:, :], A["L0_gnn_W_b"].rearrange("(f o) -> f o", o=1))
                load(a_col[:, :], A["L0_gnn_a"])
                load(fcw[:, :], A["L1_gnn_fc_w"])
                load(C["fc"][F:F + 1, :], A["L1_gnn_fc_b"].rearrange("(o f) -> o f", o=1), s["rows"])
                for i in range(5):
                    load(D["rows"][i][ZERO_ROW:ZERO_ROW + 1, :], zrow[:, :], s["rows"])
                sp.wait_ge(s["v"], mark["f"])
                sets = D["row_sets"]
                for row, i in ((D["same"], 0), (D["f2"], 6), (sets[0][:, 1, :], 0), (sets[0][:, 2, :], 5),
                               (sets[1][:, 1, :], 0), (sets[1][:, 2, :], 6)):
                    load(row.rearrange("o (p c) -> (o p) c", c=256), q[:, i, :], s["rows"])
                sp.wait_ge(s["rows"], 12 * 16)

            @block.tensor
            def _(pe):
                pe.wait_ge(s["v"], mark["scan"])
                pe.matmul(bank[0][0:1, 0:HALF], q[:, 4, 255:256], C["ident"][0:HALF, 0:HALF], start=True, stop=True)
                pe.matmul(bank[0][0:1, 128:128 + HALF], q[:, 3, 255:256], C["ident"][0:HALF, 0:HALF],
                          start=True, stop=True).then_inc(s["pe"], 1)
                pe.wait_ge(s["v"], mark["carry"])
                pe.matmul(bank[1][0:HALF, 0:1], carry[0:1, 0:HALF], ones[0:1, 0:1],
                          start=True, stop=True).then_inc(s["pe"], 1)
                for i, a in enumerate((ef[:, 0, :], ef[:, 1, :], q[:, 2, :], q[:, 1, :])):
                    for j in range(2):
                        last = pe.transpose(bank[2 + i][:, 128 * j:128 * j + HALF], a[:, 128 * j:128 * j + P],
                                            C["ident"][0:HALF, 0:HALF])
                last.then_inc(s["pe"], 1)
                pe.wait_ge(s["v"], mark["a"])
                pe.wait_ge(s["weights"], NW * 16)
                pe.transpose(bank[6][0:96, 0:F], wm[:, 0:96], C["ident"][0:F, 0:F])
                pe.transpose(bank[6][0:F, 64:128], wm[:, 96:160], C["ident"][0:F, 0:F])
                pe.transpose(bank[6][0:F, 128:192], fcw[:, :], C["ident"][0:F, 0:F])
                pe.matmul(bank[6][0:96, 256:384], ww[:, 0:96], a_rep[:, :], start=True, stop=True)
                pe.matmul(bank[6][0:F, 384:512], ww[:, 96:160], a_rep[:, :], start=True, stop=True)
                pe.matmul(bank[7][:, 0:1], a_rep[:, :], wb[:, :], start=True, stop=True).then_inc(s["pe"], 1)

            @block.scalar
            def _(act):
                act.wait_ge(s["v"], mark["count"])
                act.activation(q[:, 5:7, :], q[:, 5:7, :], ACT.Sqrt).then_inc(s["evac"], 1)
    return H


def tile_rows(a, g):
    return a[bass.ds(g.at() * W, W), :].rearrange("(t p) f -> p t f", p=P)


def table_phase(K, outer, H):
    nc, A, C, D, bank = K["nc"], K["A"], K["C"], K["D"], K["bank"]
    with Phase(nc) as ctx:
        def sb(name, shape, dt=F32):
            return ctx.enter_context(nc.sbuf_tensor(name, shape, dt))
        R = 4
        s_hi = sb("s_hi", [P, R, HI], F16)
        s_lo = sb("s_lo", [P, R, LO], F16)
        d_h1 = sb("d_h1", [P, R, HI], F16)
        d_h2 = sb("d_h2", [P, R, HI], F16)
        d_lo = sb("d_lo", [P, R, LO], F16)
        tab = sb("tab", [HALF, 2, LO, 2])
        val = sb("val", [HALF, 2, LO])
        zero = sb("zero", [HALF, 2, LO])
        deg = sb("deg", [HALF, 2, LO])
        ring = sb("x_ring", [P, 2, GT * F])
        idx_ring = sb("x_idx_ring", [P, 2, GT], I32)
        s = sems(nc, ctx, "tb", "hot counted v rooted stored indexed gathered:2 kept:2 passed")
        with nc.Block() as block:
            @block.vector
            def _(v):
                def hot(g):
                    k = g.ring(R)
                    t = g.at()
                    need(v, s["counted"], g.at(-R + 1), TILES)
                    def col(a):
                        return a[:, bass.ds(t, 1)]
                    v.tensor_scalar(s_hi[:, k, :], H["io"][:, 0:HI], col(H["shi"]), None, ALU.is_equal)
                    v.tensor_scalar(s_lo[:, k, :], H["io"][:, :], col(H["slo"]), None, ALU.is_equal)
                    v.tensor_scalar(d_h1[:, k, :], H["io"][:, 0:HI], col(H["dhi"]), col(H["w1"]), ALU.is_equal, ALU.mult)
                    v.tensor_scalar(d_h2[:, k, :], H["io"][:, 0:HI], col(H["dhi"]), col(H["w2"]), ALU.is_equal, ALU.mult)
                    v.tensor_scalar(d_lo[:, k, :], H["io"][:, :], col(H["dlo"]), None, ALU.is_equal) \
                        .then_inc(s["hot"], 1)
                pipeline(v, TILES, [(0, hot)])
                v.wait_ge(s["counted"], TILES)
                n = [0]

                def link(ins):
                    n[0] += 1
                    ins.then_inc(s["v"], 1)
                    v.wait_ge(s["v"], n[0])
                for m in range(2):
                    link(v.tensor_scalar(deg[:, m, :], bank[m][0:HALF, :], 1.0, None, ALU.max))
                for m in range(2):
                    link(v.tensor_copy(val[:, m, :], bank[2 + m][0:HALF, :]))
                link(v.tensor_scalar(zero[:, :, :], val[:, :, :], 0.0, float(ZERO_ROW), ALU.is_equal, ALU.mult))
                link(v.tensor_scalar(val[:, :, :], val[:, :, :], float(P), 0.0, ALU.subtract, ALU.max))
                link(v.tensor_tensor(tab[:, :, :, 0], val[:, :, :], zero[:, :, :], ALU.add))
                v.wait_ge(s["rooted"], 1)
                link(v.reciprocal(tab[:, :, :, 1], deg[:, :, :]))

            @block.scalar
            def _(act):
                act.wait_ge(s["v"], 2)
                act.activation(deg[:, :, :], deg[:, :, :], ACT.Sqrt).then_inc(s["rooted"], 1)

            @block.tensor
            def _(pe):
                def count(g):
                    k = g.ring(R)
                    first = isinstance(g.at(), int) and g.at() == 0
                    final = isinstance(g.at(), int) and g.at() == TILES - 1
                    pe.wait_ge(s["hot"], g.at(1))
                    for m in range(2):
                        part = slice(m * HALF, m * HALF + HALF)
                        pe.matmul(bank[m][0:HALF, :], s_hi[:, k, part], s_lo[:, k, :], start=first, stop=final,
                                  skip_group_check=True)
                        pe.matmul(bank[2 + m][0:HALF, :], d_h1[:, k, part], d_lo[:, k, :], start=first,
                                  stop=False, skip_group_check=True)
                        last = pe.matmul(bank[2 + m][0:HALF, :], d_h2[:, k, part], d_lo[:, k, :], start=False,
                                         stop=final, skip_group_check=True)
                    last.then_inc(s["counted"], 1)
                pipeline(pe, TILES, [(0, count)])

            @block.gpsimd
            def _(g):
                gather(s, g, K["A"]["x"], N, C["src"], ring, idx_ring, GT, F, s["kept"], 16)

            @block.sync
            def _(sp):
                def keep(g):
                    k = g.ring(2)
                    sp.wait_ge(s["gathered"][k], g.turn(2) * (16 * GT) + 16 * GT)
                    sp.dma_start(tile_rows(D["xs"], g), ring[:, k, :].rearrange("p (t f) -> p t f", f=F)) \
                        .then_inc(s["kept"][k], 16)
                pipeline(sp, GROUPS, [(0, keep)])
                for k in range(2):
                    sp.wait_ge(s["kept"][k], (GROUPS - k + 1) // 2 * 16)
                sp.wait_ge(s["v"], 8)
                sp.dma_start(D["table"].rearrange("(m p l) c -> p m l c", m=2, p=HALF), tab[:, :, :, :]) \
                    .then_inc(s["stored"], 16)
                sp.wait_ge(s["stored"], 16)


CENTER_LAG = {1: 1, 2: 2, 3: 4}
NORM_LAG = {1: 2, 2: 3, 3: 5}
CONV_LAG = {2: 4, 3: 6}
OUT_LAG = 7


def unit_phase(K, kind):
    nc, A, C, D, bank = K["nc"], K["A"], K["C"], K["D"], K["bank"]
    node, source = kind == "node", kind == "src"
    n = NODE_UNITS if node else EDGE_UNITS
    norms = (1,) if kind == "dst" else (1, 2, 3)
    convs = () if kind == "dst" else (2, 3)
    with Phase(nc) as ctx:
        def sb(name, r, shape=W, dt=F32):
            return ctx.enter_context(nc.sbuf_tensor(f"{kind}_{name}", [P, r, shape], dt))

        x_in, xT, h1, x2, h2, res = sb("x_in", 4), sb("xT", 2), sb("h1", 2), sb("x2", 4), sb("h2", 2), sb("res", 2)
        act2, x3, h3, act3, y, x4, rows = (sb("act2", 2), sb("x3", 4), sb("h3", 2), sb("act3", 2), sb("y", 1),
                                           sb("x4", 2), sb("rows", 2))
        square, std, rstd = (sb(a, 3) for a in ("square", "std", "rstd"))
        h, act = {1: h1, 2: h2, 3: h3}, {2: act2, 3: act3}
        s = sems(nc, ctx, kind, "loaded:4 turned xT x2 res x3 y x4 outT out_rows stored:2 centered:n squared:n "
                 "var:n std:n rstd:n h:n conv1:n act:n conv2:n indexed gathered:2 kept:2 passed looked:2 copied")
        kept = []
        if source:
            kept = [(h1, NORM_LAG[1], s["h"][1], D["src_pairs"][0]), (h2, NORM_LAG[2], s["h"][2], D["src_pairs"][1]),
                    (act2, CONV_LAG[2], s["act"][2], D["src_pairs"][2]), (h3, NORM_LAG[3], s["h"][3], D["src_pairs"][3]),
                    (act3, CONV_LAG[3], s["act"][3], D["src_pairs"][4])]
        elif not node:
            kept = [(xT, 0, s["xT"], D["dst_pairs"][0]), (h1, NORM_LAG[1], s["h"][1], D["dst_pairs"][1])]
        kept_sem = [[one(f"{kind}_kept{i}_{k}", ctx, nc) for k in range(2)]
                    for i in range(len(kept))]

        if node:
            fetch_ring = sb("fetch_ring", 2, 2 * F)
            idx_ring = sb("idx_ring", 2, 4, I32)
            tab_ring = sb("tab_ring", 2, 2 * GT)

        def free_of_store(eng, buf, g):
            for i, item in enumerate(kept):
                if item[0] is buf:
                    need(eng, kept_sem[i][g.ring(2)], g.turn(2) * 16)

        def start(g, rows_in_all, per, total):
            u = g.at()
            return total - per if isinstance(u, int) and u == n - 1 else u * per

        def node_rows(a, g):
            return a[bass.ds(start(g, N, UR, N), UR), :].rearrange("(p r) f -> p r f", r=UR // P)

        def edge_rows(a, g):
            return a[bass.ds(start(g, EPAD, UR, EPAD), UR), :].rearrange("(t p) f -> p t f", p=P)

        with nc.Block() as block:
            @block.sync
            def _(sp):
                def load(g):
                    need(sp, s["turned"], g.at(-3), n)
                    src = node_rows(A["x"], g) if node else edge_rows(D["xs"] if source else D["xd"], g)
                    sp.dma_start(x_in[:, g.ring(4), :].rearrange("p (r f) -> p r f", f=F), src) \
                        .then_inc(s["loaded"][g.ring(4)], 16)

                def keep(i):
                    buf, lag, made, pairs = kept[i]

                    def part(g):
                        sp.wait_ge(made, g.at(1))
                        at = start(g, 0, GT, TILES // 2)
                        if isinstance(g.at(), int) and g.at() == n - 1:
                            sp.wait_ge(kept_sem[i][(n - 2) % 2], n // 2 * 16)
                        sp.dma_start(pairs[bass.ds(at, GT), :, :].rearrange("q r c -> r q c"),
                                     buf[:, g.ring(2), :].rearrange("p (q c) -> p q c", c=P)) \
                            .then_inc(kept_sem[i][g.ring(2)], 16)
                    return lag + 2, part

                def write(g):
                    sp.wait_ge(s["out_rows"], g.at(1))
                    if isinstance(g.at(), int) and g.at() == n - 1:
                        sp.wait_ge(s["stored"][(n - 2) % 2], n // 2 * 16)
                    sp.dma_start(node_rows(K["out"], g), rows[:, g.ring(2), :].rearrange("p (r f) -> p r f", f=F)) \
                        .then_inc(s["stored"][g.ring(2)], 16)

                def store_fetched(g):
                    sp.wait_ge(s["gathered"][g.ring(2)], g.turn(2) * 32 + 32)
                    sp.dma_start(D["xd"][bass.ds(g.at() * 2 * P, 2 * P), :].rearrange("(t p) f -> p t f", p=P),
                                 fetch_ring[:, g.ring(2), :].rearrange("p (t f) -> p t f", f=F)) \
                        .then_inc(s["kept"][g.ring(2)], 16)

                parts = [(0, load)] + [keep(i) for i in range(len(kept))]
                if node:
                    parts += [(3, store_fetched), (OUT_LAG + 2, write)]
                pipeline(sp, n, parts)
                for k in range(2):
                    for i in range(len(kept)):
                        sp.wait_ge(kept_sem[i][k], (n - k + 1) // 2 * 16)
                    if node:
                        sp.wait_ge(s["stored"][k], (n - k + 1) // 2 * 16)
                        sp.wait_ge(s["kept"][k], (n - k + 1) // 2 * 16)

            if node:

                @block.gpsimd
                def _(g):
                    gather(s, g, A["x"], N, C["dst"], fetch_ring, idx_ring, 2, F, s["kept"], 16)
                    look_up(K, s, g, tab_ring, idx_ring)

            @block.tensor
            def _(pe):
                def turn(g):
                    pe.wait_ge(s["loaded"][g.ring(4)], g.turn(4) * 16 + 16)
                    need(pe, s["xT"], g.at(), n)
                    for j in range(GT):
                        last = pe.transpose(bank[0][:, j * P:j * P + P], x_in[:, g.ring(4), j * P:j * P + P],
                                            C["ident"][:, :])
                    last.then_inc(s["turned"], 1)

                def center(i, src, ready, r):
                    def part(g):
                        pe.wait_ge(ready, g.at(1))
                        need(pe, s["h"][i], g.at())
                        pe.matmul(bank[i][:, :], C["center"][:, :], src[:, g.ring(r), :], start=True, stop=True) \
                            .then_inc(s["centered"][i], 1)
                    return CENTER_LAG[i], part

                def variance(i):
                    def part(g):
                        pe.wait_ge(s["squared"][i], g.at(1))
                        for j in norms:
                            need(pe, s["std"][j], g.at(NORM_LAG[i] - NORM_LAG[j] + (1 if j < i else 0)), n)
                        pe.matmul(bank[4][:, :], C["mean"][:, :], square[:, i - 1, :], start=True, stop=True) \
                            .then_inc(s["var"][i], 1)
                    return NORM_LAG[i], part

                def conv1(i):
                    def part(g):
                        pe.wait_ge(s["h"][i], g.at(1))
                        for j in convs:
                            need(pe, s["act"][j], g.at(CONV_LAG[i] - CONV_LAG[j] + (1 if j < i else 0)), n)
                        pe.matmul(bank[5][:, :], C["wconv"][:, 2 * i - 4, :], h[i][:, g.ring(2), :],
                                  start=True, stop=True).then_inc(s["conv1"][i], 1)
                    return CONV_LAG[i], part

                def conv2(i):
                    def part(g):
                        pe.wait_ge(s["act"][i], g.at(1))
                        need(pe, s["x3"], g.at(CONV_LAG[i] - CONV_LAG[2] + (1 if i > 2 else 0)), n)
                        if node:
                            need(pe, s["y"], g.at(CONV_LAG[i] - CONV_LAG[3]), n)
                        pe.matmul(bank[6][:, :], C["wconv"][:, 2 * i - 3, :], act[i][:, g.ring(2), :],
                                  start=True, stop=True).then_inc(s["conv2"][i], 1)
                    return CONV_LAG[i], part

                def turn_back(g):
                    pe.wait_ge(s["x4"], g.at(1))
                    need(pe, s["out_rows"], g.at())
                    for j in range(GT):
                        last = pe.transpose(bank[7][:, j * P:j * P + P], x4[:, g.ring(2), j * P:j * P + P],
                                            C["ident"][:, :])
                    last.then_inc(s["outT"], 1)

                parts = [variance(1)]
                if convs:
                    parts += [conv1(2), variance(2), conv2(2), variance(3), conv1(3)]
                parts += [(OUT_LAG, turn_back)] if node else []
                parts += [(0, turn)]
                parts += [conv2(3)] if node else []
                parts += [center(1, xT, s["xT"], 2)]
                if convs:
                    parts += [center(2, x2, s["x2"], 4), center(3, x3, s["x3"], 4)]
                pipeline(pe, n, parts)

            @block.scalar
            def _(act_):
                act_.preload_act_table_set("natural_log_exp_and_others")

                def copy_x(g):
                    act_.wait_ge(s["turned"], g.at(1))
                    need(act_, s["centered"][1], g.at(-1), n)
                    if convs:
                        need(act_, s["x2"], g.at(-1), n)
                    free_of_store(act_, xT, g)
                    act_.activation(xT[:, g.ring(2), :], bank[0][:, :], ACT.Copy).then_inc(s["xT"], 1)

                def squares(i):
                    def part(g):
                        act_.wait_ge(s["centered"][i], g.at(1))
                        need(act_, s["var"][i], g.at())
                        act_.activation(square[:, i - 1, :], bank[i][:, :], ACT.Square).then_inc(s["squared"][i], 1)
                    return CENTER_LAG[i], part

                def log_var(i):
                    def part(g):
                        act_.wait_ge(s["var"][i], g.at(1))
                        need(act_, s["rstd"][i], g.at())
                        act_.activation(std[:, i - 1, :], bank[4][:, :], ACT.Ln, bias=C["eps"][:, 0:1]) \
                            .then_inc(s["std"][i], 1)
                    return NORM_LAG[i], part

                def deviation(i):
                    def part(g):
                        act_.wait_ge(s["std"][i], g.at(1))
                        need(act_, s["h"][i], g.at())
                        act_.activation(rstd[:, i - 1, :], std[:, i - 1, :], ACT.Exp, scale=-0.5) \
                            .then_inc(s["rstd"][i], 1)
                    return NORM_LAG[i], part

                def relu(i):
                    def part(g):
                        act_.wait_ge(s["conv1"][i], g.at(1))
                        if i == 2 or node:
                            need(act_, s["conv2"][i], g.at(-1))
                        free_of_store(act_, act[i], g)
                        act_.activation(act[i][:, g.ring(2), :], bank[5][:, :], ACT.Relu,
                                        bias=C["bias"][:, 2 * i - 4:2 * i - 3]).then_inc(s["act"][i], 1)
                    return CONV_LAG[i], part

                def copy_out(g):
                    act_.wait_ge(s["outT"], g.at(1))
                    need(act_, s["stored"][g.ring(2)], g.turn(2) * 16)
                    act_.activation(rows[:, g.ring(2), :], bank[7][:, :], ACT.Copy).then_inc(s["out_rows"], 1)

                parts = [log_var(1)]
                if convs:
                    parts += [relu(2), deviation(1), log_var(2), deviation(2), log_var(3), relu(3), deviation(3)]
                else:
                    parts += [deviation(1)]
                parts += [(OUT_LAG, copy_out)] if node else []
                parts += [(0, copy_x)] + [squares(i) for i in norms]
                pipeline(act_, n, parts)

            @block.vector
            def _(v):
                reads = {1: bool(convs), 2: True, 3: node}

                def normalise(i):
                    def part(g):
                        v.wait_ge(s["rstd"][i], g.at(1))
                        if i > 1:
                            need(v, s["conv1"][i], g.at(-1), n)
                        free_of_store(v, h[i], g)
                        need(v, {1: s["x2"], 2: s["res"], 3: s["y"]}[i] if reads[i] else s["h"][i], g.at(-1), n)
                        v.scalar_tensor_tensor(h[i][:, g.ring(2), :], bank[i][:, :], 0.0, rstd[:, i - 1, :],
                                               ALU.max, ALU.mult).then_inc(s["h"][i], 1)
                        if i == 1 and convs:
                            v.wait_ge(s["h"][1], g.at(1))
                            need(v, s["centered"][2], g.at(-3), n)
                            need(v, s["res"], g.at(-3), n)
                            v.tensor_tensor(x2[:, g.ring(4), :], xT[:, g.ring(2), :], h1[:, g.ring(2), :],
                                            ALU.add).then_inc(s["x2"], 1)
                        if i == 2:
                            v.wait_ge(s["h"][2], g.at(1))
                            v.wait_ge(s["x2"], g.at(1))
                            need(v, s["x3"], g.at(-1), n)
                            v.tensor_tensor(res[:, g.ring(2), :], x2[:, g.ring(4), :], h2[:, g.ring(2), :],
                                            ALU.add).then_inc(s["res"], 1)
                    return NORM_LAG[i], part

                def layer2(g):
                    v.wait_ge(s["conv2"][2], g.at(1))
                    v.wait_ge(s["res"], g.at(1))
                    need(v, s["centered"][3], g.at(-3), n)
                    if node:
                        need(v, s["x4"], g.at(-3), n)
                    v.scalar_tensor_tensor(x3[:, g.ring(4), :], bank[6][:, :], C["bias"][:, 1:2],
                                           res[:, g.ring(2), :], ALU.add, ALU.add).then_inc(s["x3"], 1)

                def layer3(g):
                    v.wait_ge(s["conv2"][3], g.at(1))
                    v.wait_ge(s["h"][3], g.at(1))
                    need(v, s["x4"], g.at())
                    v.scalar_tensor_tensor(y[:, 0, :], bank[6][:, :], C["bias"][:, 3:4], h3[:, g.ring(2), :],
                                           ALU.add, ALU.add).then_inc(s["y"], 1)
                    v.wait_ge(s["y"], g.at(1))
                    v.wait_ge(s["x3"], g.at(1))
                    need(v, s["outT"], g.at(-1), n)
                    v.scalar_tensor_tensor(x4[:, g.ring(2), :], y[:, 0, :], 0.0, x3[:, g.ring(4), :],
                                           ALU.max, ALU.add).then_inc(s["x4"], 1)

                parts = [normalise(1)]
                if convs:
                    parts += [(CONV_LAG[2], layer2), normalise(2), normalise(3)]
                if node:
                    parts += [(CONV_LAG[3], layer3)]
                pipeline(v, n, parts)


def gather(s, eng, table, rows, idx, ring, idx_ring, per, width, reader, count):
    def fetch(g):
        k = g.ring(2)
        pool_need(eng, s, reader[k], g.turn(2) * count)
        eng.tensor_copy(idx_ring[:, k, 0:per], idx[:, bass.ds(g.at() * per, per)]).then_inc(s["indexed"], 1)
        pool_need(eng, s, s["indexed"], g.at(1))
        for j in range(per):
            eng.indirect_dma_start(
                out=ring[:, k, j * width:(j + 1) * width], out_offset=None, in_=table,
                in_offset=bass.IndirectOffsetOnAxis(ap=idx_ring[:, k, j:j + 1], axis=0),
                bounds_check=rows - 1, oob_is_err=False).then_inc(s["gathered"][k], 16)
    pipeline(eng, TILES // per, [(0, fetch)])
    for k in range(2):
        eng.wait_ge(s["gathered"][k], (TILES // per - k + 1) // 2 * 16 * per)


def look_up(K, s, eng, ring, idx_ring):
    C = K["C"]

    def fetch(g):
        k = g.ring(2)
        pool_need(eng, s, s["copied"], g.at(-1) * 2)
        eng.tensor_copy(idx_ring[:, k, :], C["src"][:, bass.ds(g.at() * GT, GT)]) \
            .then_inc(s["indexed"], 1)
        pool_need(eng, s, s["indexed"], g.at(TILES // 2 + 1))
        for j in range(GT):
            eng.indirect_dma_start(
                out=ring[:, k, 2 * j:2 * j + 2], out_offset=None, in_=K["D"]["table"],
                in_offset=bass.IndirectOffsetOnAxis(ap=idx_ring[:, k, j:j + 1], axis=0),
                bounds_check=HI * LO - 1, oob_is_err=False).then_inc(s["looked"][k], 16)

    def copy(g):
        k = g.ring(2)
        pool_need(eng, s, s["looked"][k], g.turn(2) * (16 * GT) + 16 * GT)
        got = ring[:, k, :].rearrange("p (t c) -> p t c", c=2)
        eng.tensor_copy(C["slotf"][:, bass.ds(g.at() * GT, GT)], got[:, :, 0]).then_inc(s["copied"], 1)
        eng.tensor_copy(C["oscale"][:, bass.ds(g.at() * GT, GT)], got[:, :, 1]).then_inc(s["copied"], 1)
    pipeline(eng, GROUPS, [(0, fetch), (1, copy)])


def mask_phase(K):
    nc, C, D, bank = K["nc"], K["C"], K["D"], K["bank"]
    with Phase(nc) as ctx:
        loc = ctx.enter_context(nc.sbuf_tensor("loc", [P, 2, TILES], F32))
        turned = ctx.enter_context(nc.sbuf_tensor("mask_rows", [HALF, 3, 2, P], F32))
        s = sems(nc, ctx, "mk", "made turned copied stored")
        with nc.Block() as block:
            @block.vector
            def _(v):
                v.tensor_copy(C["slot"][:, :], C["slotf"][:, :])
                v.tensor_scalar(loc[:, 0, :], C["slotf"][:, :], float(ZERO_ROW), None, ALU.is_equal).then_inc(s["made"], 1)
                v.wait_ge(s["made"], 1)
                v.tensor_tensor(loc[:, 1, :], loc[:, 0, :], C["oscale"][:, :], ALU.mult).then_inc(s["made"], 1)
                v.wait_ge(s["turned"], 1)
                for i in range(3):
                    last = v.tensor_copy(turned[:, i, :, :].rearrange("p j c -> p (j c)"), bank[i][0:HALF, 0:2 * P])
                last.then_inc(s["copied"], 1)

            @block.tensor
            def _(pe):
                pe.wait_ge(s["made"], 2)
                for i, a in enumerate((loc[:, 0, :], loc[:, 1, :], C["oscale"][:, :])):
                    for j in range(2):
                        last = pe.transpose(bank[i][0:HALF, j * P:j * P + P], a[:, j * HALF:(j + 1) * HALF],
                                            C["ident"][:, :])
                last.then_inc(s["turned"], 1)

            @block.sync
            def _(sp):
                sp.wait_ge(s["copied"], 1)
                for i, row in enumerate((D["row_sets"][1][:, 0, :], D["row_sets"][0][:, 0, :], D["osc"])):
                    sp.dma_start(row.rearrange("o (j t c) -> (o t) j c", j=2, t=HALF), turned[:, i, :, :]) \
                        .then_inc(s["stored"], 16)
                sp.wait_ge(s["stored"], 48)


def pair_cols(pairs, g):
    return pairs[bass.ds(g.at() * (GT // 2), GT // 2), :, :].rearrange("q (h f) n -> f (q h) n", h=2)


def cols(a, g):
    return a[:, bass.ds(g.at() * W, W)]


def spread(row, g, partitions):
    return row[:, bass.ds(g.at() * W, W)].broadcast_to([partitions, W])


def attention_phase(K):
    nc, A, C, D, bank = K["nc"], K["A"], K["C"], K["D"], K["bank"]
    n = GROUPS
    with Phase(nc) as ctx:
        def sb(name, p, r, w=W):
            return ctx.enter_context(nc.sbuf_tensor(f"at_{name}", [p, r, w], F32))

        feat, xd, hd, same = sb("feat", P, 4), sb("xd", F, 4), sb("hd", F, 4), sb("same", P, 4)
        edge_in = sb("edge_in", P, 4, GT * 64)
        seam, z, logit, peak = sb("seam", P, 2), sb("z", P, 2), sb("logit", P, 2), sb("peak", P, 2, W + 1)
        da, db = sb("da", P, 2), sb("db", P, 2)
        decay, weight = sb("decay", P, 2), sb("weight", P, 2)
        part, total = sb("part", P, 2), sb("total", P, 2)
        lnsum, inv, scaled, agg, relu = (sb(a, F, 2) for a in ("lnsum", "inv", "scaled", "agg", "relu"))
        x1, square, std, rstd, h1, res = (sb(a, F, 4 if a == "x1" else 2) for a in
                                            ("x1", "square", "std", "rstd", "h1", "res"))
        rows = sb("rows", P, 2, GT * F)
        s = sems(nc, ctx, "at", "filled loaded:4 loaded_x:4 edge_turned edge_copied seam logits z logit peak peak_in da db dd decay "
                 "weight part total mixed lnsum inv scaled agg relu x1 centered squared var std rstd h1 res "
                 "turned rows res_stored:2 rows_stored:2 pe_passed")
        with nc.Block() as block:
            @block.sync
            def _(sp):
                def load(g):
                    k = g.ring(4)
                    need(sp, s["part"], g.at(-3), n)
                    need(sp, s["logits"], g.at(-3), n)
                    need(sp, s["edge_turned"], g.at(-3), n)
                    need(sp, s["mixed"], g.at(-3), n)
                    need(sp, s["seam"], g.at(-3), n)
                    def get(dst, src):
                        sp.dma_start(dst, src).then_inc(s["loaded"][k], 16)
                    get(feat[0:F, k, :].rearrange("p (t c) -> p t c", c=P), pair_cols(D["src_pairs"][0], g))
                    get(hd[:, k, :].rearrange("p (t c) -> p t c", c=P), pair_cols(D["dst_pairs"][1], g))
                    get(same[:, k, :], spread(D["same"], g, P))
                    e = edge_in[:, k, :].rearrange("p (t f) -> p t f", f=64)
                    if isinstance(g.at(), int) and g.at() == n - 1:
                        whole = (E - (n - 1) * W) // P
                        at = (n - 1) * W
                        get(e[:, 0:whole, 0:EF],
                            A["edge_attr_32"][at:at + whole * P, :].rearrange("(t p) f -> p t f", p=P))
                        get(e[0:E - at - whole * P, whole, 0:EF], A["edge_attr_32"][at + whole * P:E, :])
                    else:
                        get(e[:, :, 0:EF],
                            A["edge_attr_32"][bass.ds(g.at() * W, W), :].rearrange("(t p) f -> p t f", p=P))

                def load_x(g):
                    k = g.ring(4)
                    need(sp, s["x1"], g.at(-3), n)
                    sp.dma_start(xd[:, k, :].rearrange("p (t c) -> p t c", c=P), pair_cols(D["dst_pairs"][0], g)) \
                        .then_inc(s["loaded_x"][k], 16)

                def keep(g):
                    k = g.ring(2)
                    sp.wait_ge(s["res"], g.at(1))
                    sp.dma_start(cols(D["res"][0], g), res[:, k, :]).then_inc(s["res_stored"][k], 16)

                def keep_rows(g):
                    k = g.ring(2)
                    sp.wait_ge(s["rows"], g.at(1))
                    sp.dma_start(tile_rows(D["rows"][0], g), rows[:, k, :].rearrange("p (t f) -> p t f", f=F)) \
                        .then_inc(s["rows_stored"][k], 16)
                sp.wait_ge(s["filled"], 1)
                pipeline(sp, n, [(8, keep_rows), (7, keep), (0, load), (2, load_x)])
                for k in range(2):
                    sp.wait_ge(s["res_stored"][k], (n - k + 1) // 2 * 16)
                    sp.wait_ge(s["rows_stored"][k], (n - k + 1) // 2 * 16)

            def loaded(g):
                return g.turn(4) * 64 + (80 if isinstance(g.at(), int) and g.at() == n - 1 else 64)

            @block.gpsimd
            def _(g):
                g.memset(edge_in[:, :, :], 1.0).then_inc(s["filled"], 1)

            @block.tensor
            def _(pe):
                def turn_edges(g):
                    k = g.ring(4)
                    pe.wait_ge(s["loaded"][k], loaded(g))
                    need(pe, s["edge_copied"], g.at())
                    pe.sem_inc(s["pe_passed"], 1)
                    for t in range(GT):
                        last = pe.matmul(bank[0][64:P, t * P:t * P + P], edge_in[:, k, t * 64:t * 64 + 64],
                                         C["ident"][:, :], start=True, stop=True)
                    last.then_inc(s["edge_turned"], 1)

                def logits(g):
                    k = g.ring(4)
                    pe.wait_ge(s["edge_copied"], g.at(1))
                    need(pe, s["z"], g.at())
                    pe.sem_inc(s["pe_passed"], 1)
                    pe.matmul(bank[1][:, :], C["v_se"][:, :], feat[0:96, k, :], start=True, stop=False)
                    pe.matmul(bank[1][:, :], C["v_d"][:, :], hd[:, k, :], start=False, stop=True).then_inc(s["logits"], 1)

                def mix(g):
                    k = g.ring(2)
                    pe.wait_ge(s["total"], g.at(1))
                    need(pe, s["agg"], g.at())
                    pe.sem_inc(s["pe_passed"], 1)
                    pe.matmul(bank[2][0:F, :], C["wm_se"][:, :], total[0:96, k, :], start=True, stop=True)
                    pe.matmul(bank[3][0:F, :], C["take_sum"][:, :], total[:, k, :], start=True, stop=True)
                    pe.matmul(bank[4][0:F, :], C["wm_d"][:, :], hd[:, g.ring(4), :], start=True, stop=True) \
                        .then_inc(s["mixed"], 1)

                def center(g):
                    pe.wait_ge(s["x1"], g.at(1))
                    need(pe, s["h1"], g.at())
                    pe.sem_inc(s["pe_passed"], 1)
                    pe.matmul(bank[5][0:F, :], C["center"][0:F, 0:F], x1[:, g.ring(4), :], start=True, stop=True) \
                        .then_inc(s["centered"], 1)

                def variance(g):
                    pe.wait_ge(s["squared"], g.at(1))
                    need(pe, s["std"], g.at())
                    pe.sem_inc(s["pe_passed"], 1)
                    pe.matmul(bank[6][0:F, :], C["mean"][0:F, 0:F], square[:, g.ring(2), :], start=True, stop=True) \
                        .then_inc(s["var"], 1)

                def turn(g):
                    pe.wait_ge(s["h1"], g.at(1))
                    need(pe, s["rows"], g.at())
                    pe.sem_inc(s["pe_passed"], 1)
                    for t in range(GT):
                        last = pe.transpose(bank[7][:, t * F:t * F + F], h1[:, g.ring(2), t * P:t * P + P],
                                            C["ident"][0:F, 0:F])
                    last.then_inc(s["turned"], 1)
                pipeline(pe, n, [(3, mix), (5, variance), (1, logits), (6, turn), (0, turn_edges), (4, center)])

            @block.scalar
            def _(act):
                act.preload_act_table_set("natural_log_exp_and_others")

                def copy_edges(g):
                    act.wait_ge(s["edge_turned"], g.at(1))
                    need(act, s["part"], g.at(-3), n)
                    need(act, s["logits"], g.at(-3), n)
                    act.activation(feat[F:P, g.ring(4), :], bank[0][F:P, :], ACT.Copy).then_inc(s["edge_copied"], 1)

                def bias_logits(g):
                    act.wait_ge(s["logits"], g.at(1))
                    need(act, s["logit"], g.at(-1), n)
                    act.activation(z[:, g.ring(2), :], bank[1][:, :], ACT.Identity, bias=C["c0"][:, 0:1]) \
                        .then_inc(s["z"], 1)

                def weights(g):
                    k = g.ring(2)
                    act.wait_ge(s["dd"], g.at(1))
                    need(act, s["total"], g.at(-1), n)
                    act.activation(decay[:, k, :], da[:, k, :], ACT.Exp).then_inc(s["decay"], 1)
                    act.wait_ge(s["db"], g.at(1))
                    need(act, s["part"], g.at(-1), n)
                    act.activation(weight[:, k, :], db[:, k, :], ACT.Exp).then_inc(s["weight"], 1)

                def invert_sum(g):
                    k = g.ring(2)
                    act.wait_ge(s["mixed"], g.at(1))
                    act.activation(lnsum[:, k, :], bank[3][0:F, :], ACT.Ln).then_inc(s["lnsum"], 1)
                    act.wait_ge(s["lnsum"], g.at(1))
                    need(act, s["scaled"], g.at(-1), n)
                    act.activation(inv[:, k, :], lnsum[:, k, :], ACT.Exp, scale=-1.0).then_inc(s["inv"], 1)

                def relu_agg(g):
                    k = g.ring(2)
                    act.wait_ge(s["agg"], g.at(1))
                    need(act, s["x1"], g.at(-1), n)
                    act.activation(relu[:, k, :], agg[:, k, :], ACT.Relu, bias=C["bias"][0:F, 4:5]).then_inc(s["relu"], 1)

                def squares(g):
                    act.wait_ge(s["centered"], g.at(1))
                    need(act, s["var"], g.at(-1), n)
                    act.activation(square[:, g.ring(2), :], bank[5][0:F, :], ACT.Square).then_inc(s["squared"], 1)

                def deviation(g):
                    k = g.ring(2)
                    act.wait_ge(s["var"], g.at(1))
                    act.activation(std[:, k, :], bank[6][0:F, :], ACT.Ln, bias=C["eps"][0:F, 0:1]).then_inc(s["std"], 1)
                    act.wait_ge(s["std"], g.at(1))
                    need(act, s["h1"], g.at(-1), n)
                    act.activation(rstd[:, k, :], std[:, k, :], ACT.Exp, scale=-0.5).then_inc(s["rstd"], 1)

                def copy_rows(g):
                    act.wait_ge(s["turned"], g.at(1))
                    need(act, s["rows_stored"][g.ring(2)], g.turn(2) * 16)
                    act.activation(rows[:, g.ring(2), :], bank[7][:, 0:GT * F], ACT.Copy).then_inc(s["rows"], 1)
                pipeline(act, n, [(3, invert_sum), (5, deviation), (1, bias_logits), (3, relu_agg), (6, copy_rows),
                                  (0, copy_edges), (4, squares), (1, weights)])

            @block.vector
            def _(v):
                def residual(g):
                    k = g.ring(2)
                    v.wait_ge(s["relu"], g.at(1))
                    v.wait_ge(s["loaded_x"][g.ring(4)], g.turn(4) * 16 + 16)
                    need(v, s["centered"], g.at(-1), n)
                    need(v, s["res"], g.at(-1), n)
                    v.tensor_tensor(x1[:, g.ring(4), :], xd[:, g.ring(4), :], relu[:, k, :], ALU.add).then_inc(s["x1"], 1)

                def sum_runs(g):
                    k = g.ring(2)
                    v.wait_ge(s["weight"], g.at(1))
                    need(v, s["total"], g.at(-1), n)
                    v.tensor_tensor(part[:, k, :], feat[:, g.ring(4), :], weight[:, k, :], ALU.mult) \
                        .then_inc(s["part"], 1)
                    v.wait_ge(s["part"], g.at(1))
                    v.wait_ge(s["decay"], g.at(1))
                    need(v, s["mixed"], g.at(-1), n)
                    need(v, s["total"], g.at())
                    first = isinstance(g.at(), int) and g.at() == 0
                    v.tensor_tensor_scan(total[:, k, :], decay[:, k, :], part[:, k, :],
                                         0.0 if first else total[:, 1 - k, W - 1:W], ALU.mult, ALU.add) \
                        .then_inc(s["total"], 1)

                def maxima(g):
                    k = g.ring(2)
                    first = isinstance(g.at(), int) and g.at() == 0
                    v.wait_ge(s["z"], g.at(1))
                    need(v, s["dd"], g.at(-1), n)
                    need(v, s["db"], g.at(-1), n)
                    v.scalar_tensor_tensor(logit[:, k, :], z[:, k, :], 0.01, z[:, k, :], ALU.mult, ALU.max) \
                        .then_inc(s["logit"], 1)
                    v.wait_ge(s["logit"], g.at(1))
                    v.wait_ge(s["seam"], g.at(1))
                    need(v, s["peak"], g.at())
                    if first:
                        v.memset(peak[:, 0, 0:1], 0.0).then_inc(s["peak_in"], 1)
                    else:
                        v.tensor_copy(peak[:, k, 0:1], peak[:, 1 - k, W:W + 1]).then_inc(s["peak_in"], 1)
                    v.tensor_tensor_scan(peak[:, k, 1:W + 1], seam[:, k, :], logit[:, k, :],
                                         0.0 if first else peak[:, 1 - k, W:W + 1], ALU.add, ALU.max) \
                        .then_inc(s["peak"], 1)
                    v.wait_ge(s["peak"], g.at(1))
                    v.wait_ge(s["peak_in"], g.at(1))
                    need(v, s["weight"], g.at(-1), n)
                    v.tensor_tensor(db[:, k, :], logit[:, k, :], peak[:, k, 1:W + 1], ALU.subtract) \
                        .then_inc(s["db"], 1)
                    need(v, s["decay"], g.at(-1), n)
                    v.tensor_tensor(da[:, k, :], seam[:, k, :], peak[:, k, 0:W], ALU.add).then_inc(s["da"], 1)
                    v.wait_ge(s["da"], g.at(1))
                    v.tensor_tensor(da[:, k, :], da[:, k, :], peak[:, k, 1:W + 1], ALU.subtract).then_inc(s["dd"], 1)

                def divide(g):
                    k = g.ring(2)
                    v.wait_ge(s["inv"], g.at(1))
                    need(v, s["agg"], g.at(-1), n)
                    v.tensor_tensor(scaled[:, k, :], bank[2][0:F, :], inv[:, k, :], ALU.mult).then_inc(s["scaled"], 1)
                    v.wait_ge(s["scaled"], g.at(1))
                    need(v, s["relu"], g.at(-1), n)
                    v.tensor_tensor(agg[:, k, :], bank[4][0:F, :], scaled[:, k, :], ALU.add).then_inc(s["agg"], 1)

                def normalise(g):
                    k = g.ring(2)
                    v.wait_ge(s["rstd"], g.at(1))
                    need(v, s["turned"], g.at(-1), n)
                    need(v, s["res"], g.at(-1), n)
                    v.scalar_tensor_tensor(h1[:, k, :], bank[5][0:F, :], 0.0, rstd[:, k, :], ALU.max, ALU.mult) \
                        .then_inc(s["h1"], 1)
                    v.wait_ge(s["h1"], g.at(1))
                    need(v, s["res_stored"][k], g.turn(2) * 16)
                    v.tensor_tensor(res[:, k, :], x1[:, g.ring(4), :], h1[:, k, :], ALU.add).then_inc(s["res"], 1)

                def seams(g):
                    k = g.ring(2)
                    v.wait_ge(s["loaded"][g.ring(4)], loaded(g))
                    need(v, s["dd"], g.at(-1), n)
                    v.tensor_scalar(seam[:, k, :], same[:, g.ring(4), :], FAR, -FAR, ALU.mult, ALU.add).then_inc(s["seam"], 1)
                pipeline(v, n, [(4, residual), (2, sum_runs), (3, divide), (5, normalise), (1, maxima), (0, seams)])


def edge_phase(K, stage):
    nc, A, C, D, bank = K["nc"], K["A"], K["C"], K["D"], K["bank"]
    n = GROUPS
    i = "BCDEF".index(stage)
    first, mid, norm, last = stage == "B", stage in "CE", stage in "BD", stage == "F"
    KR = F + 1 if first else F
    weight = C["fc"][:, :] if first else C["wconv"][0:F, i - 1, 0:F]
    bias = None if first else C["bias"][0:F, i - 1:i]
    with Phase(nc) as ctx:
        def sb(name, p, r, w=W, dt=F32):
            return ctx.enter_context(nc.sbuf_tensor(f"{stage}_{name}", [p, r, w], dt))

        ring, idx_ring = sb("ring", P, 2, GT * F), sb("idx_ring", P, 2, GT, I32)
        sent_idx = sb("sent_idx", P, 2, GT, I32)
        own, nfactor, before, base, h3in = (sb(a, F, 4) for a in ("own", "nfactor", "before", "base", "h3in"))
        sets = ctx.enter_context(nc.sbuf_tensor(f"{stage}_sets", [KR, 4, 3, W], F32))
        local, same, factor = sets[0:F, :, 0, :], sets[:, :, 1, :], sets[0:F, :, 2, :]
        given, part = sb("given", F, 2), sb("part", KR, 4)
        total, full, scaled, x, y = sb("total", KR, 2), sb("full", F, 2), sb("scaled", F, 2), sb("x", F, 4), sb("y", F, 2)
        square, std, rstd, h, hs, res = (sb(a, F, 2) for a in ("square", "std", "rstd", "h", "hs", "res"))
        SCALE = 4 if norm else 3
        TURN_BACK = SCALE + 1 if not last else 3
        gs = sb("gs", P, 2, GT * F)
        rows = sb("rows", P, 2, GT * F)
        s = sems(nc, ctx, stage, "indexed gathered:2 passed loaded:4 loaded_late:4 gs turned given part total full product scaled y x "
                 "centered squared var std rstd h hs res turned_back rows kept:2 kept_x:4 rows_stored:2 sent:2 sent_indexed "
                 "pe_passed")
        NL = 2 + 1 + norm + 2 * last
        src_turned = gs if first else ring
        hs_buf = x if last else hs
        made_last = s["x"] if last else s["hs"]
        kept = [] if last else [(hs, s["hs"], D["own"][i])]
        if first:
            kept.append((res, s["res"], D["res"][1]))
        if stage == "D":
            kept.append((h, s["h"], D["h3"]))

        def kept_free(eng, g):
            if kept:
                need(eng, s["kept"][g.ring(2)], g.turn(2) * (16 * len(kept)))

        with nc.Block() as block:
            @block.sync
            def _(sp):
                def load(g):
                    k = g.ring(4)
                    need(sp, s["given"], g.at(-3), n)
                    need(sp, s["total"], g.at(-3), n)
                    need(sp, s["scaled"], g.at(-3), n)
                    need(sp, s["hs"] if mid else s["x"], g.at(-3), n)
                    if not first:
                        need(sp, s["full"], g.at(-3), n)
                    def get(dst, src):
                        sp.dma_start(dst, src).then_inc(s["loaded"][k], 16)
                    get(own[:, k, :].rearrange("p (t c) -> p t c", c=P), pair_cols(D["src_pairs"][i], g))
                    get(sets[:, k, :, :], D["row_sets"][0 if first else 1][:, :, bass.ds(g.at() * W, W)]
                        .broadcast_to([KR, 3, W]))
                    if first:
                        get(part[F:F + 1, k, :], D["osc"][:, bass.ds(g.at() * W, W)])
                    else:
                        get(before[:, k, :], cols(D["own"][i - 1], g))
                    if norm:
                        get(base[:, k, :], cols(D["res"][0 if first else 1], g))
                    if last:
                        get(base[:, k, :], cols(D["res"][2], g))
                        get(h3in[:, k, :], cols(D["h3"], g))

                def load_late(g):
                    k = g.ring(4)
                    need(sp, s["hs"], g.at(-3), n)
                    sp.dma_start(nfactor[:, k, :], spread(D["f2"], g, F)).then_inc(s["loaded_late"][k], 16)

                def keep(g):
                    k = g.ring(2)
                    for buf, made, at in kept:
                        sp.wait_ge(made, g.at(1))
                        sp.dma_start(cols(at, g), buf[:, k, :]).then_inc(s["kept"][k], 16)

                def keep_x(g):
                    k = g.ring(4)
                    sp.wait_ge(s["x"], g.at(1))
                    sp.dma_start(cols(D["res"][2], g), x[:, k, :]).then_inc(s["kept_x"][k], 16)

                def keep_rows(g):
                    k = g.ring(2)
                    sp.wait_ge(s["rows"], g.at(1))
                    sp.dma_start(tile_rows(D["rows"][i + 1], g), rows[:, k, :].rearrange("p (t f) -> p t f", f=F)) \
                        .then_inc(s["rows_stored"][k], 16)
                parts = [] if last else [(TURN_BACK + 2, keep_rows), (SCALE + 2, keep)]
                pipeline(sp, n, ([(4, keep_x)] if stage == "D" else []) + parts + [(0, load)]
                         + ([(2, load_late)] if norm else []))
                if stage == "D":
                    for k in range(4):
                        sp.wait_ge(s["kept_x"][k], (n - k + 3) // 4 * 16)
                if not last:
                    for k in range(2):
                        sp.wait_ge(s["kept"][k], (n - k + 1) // 2 * 16 * len(kept))
                        sp.wait_ge(s["rows_stored"][k], (n - k + 1) // 2 * 16)

            def loaded(g):
                return g.turn(4) * (16 * NL) + 16 * NL

            @block.gpsimd
            def _(gp):
                def fetch(g):
                    k = g.ring(2)
                    pool_need(gp, s, s["gs"] if first else s["turned"], g.at(-1))
                    gp.tensor_copy(idx_ring[:, k, :], C["slot"][:, bass.ds(g.at() * GT, GT)]).then_inc(s["indexed"], 1)
                    pool_need(gp, s, s["indexed"], g.at(1))
                    for j in range(GT):
                        gp.indirect_dma_start(
                            out=ring[:, k, j * F:(j + 1) * F], out_offset=None, in_=D["rows"][i],
                            in_offset=bass.IndirectOffsetOnAxis(ap=idx_ring[:, k, j:j + 1], axis=0),
                            bounds_check=EPAD, oob_is_err=False).then_inc(s["gathered"][k], 16)

                def send(g):
                    k = g.ring(2)
                    pool_need(gp, s, s["sent"][k], g.turn(2) * (16 * GT))
                    gp.tensor_copy(sent_idx[:, k, :], C["scat"][:, bass.ds(g.at() * GT, GT)]).then_inc(s["sent_indexed"], 1)
                    pool_need(gp, s, s["sent_indexed"], g.at(1))
                    pool_need(gp, s, s["rows"], g.at(1))
                    for j in range(GT):
                        gp.indirect_dma_start(
                            out=K["out"], out_offset=bass.IndirectOffsetOnAxis(ap=sent_idx[:, k, j:j + 1], axis=0),
                            in_=rows[:, k, j * F:(j + 1) * F], in_offset=None,
                            bounds_check=N - 1, oob_is_err=False).then_inc(s["sent"][k], 16)
                pipeline(gp, n, [(0, fetch)] + ([(TURN_BACK + 1, send)] if last else []))
                if last:
                    for k in range(2):
                        gp.wait_ge(s["sent"][k], (n - k + 1) // 2 * 16 * GT)

            @block.tensor
            def _(pe):
                def turn(g):
                    k = g.ring(2)
                    if first:
                        pe.wait_ge(s["gs"], g.at(1))
                    else:
                        pe.wait_ge(s["gathered"][k], g.turn(2) * (16 * GT) + 16 * GT)
                    need(pe, s["part"], g.at(-1), n)
                    pe.sem_inc(s["pe_passed"], 1)
                    for t in range(GT):
                        fin = pe.transpose(bank[k][0:F, t * P:t * P + P], src_turned[:, k, t * F:t * F + F],
                                           C["ident"][:, :])
                    fin.then_inc(s["turned"], 1)

                def product(g):
                    k = g.ring(2)
                    pe.wait_ge(s["total"] if first else s["full"], g.at(1))
                    need(pe, s["scaled"], g.at(-1), n)
                    pe.sem_inc(s["pe_passed"], 1)
                    pe.matmul(bank[2 + k][0:F, :], weight, (total if first else full)[:, k, :],
                              start=True, stop=True).then_inc(s["product"], 1)

                def center(g):
                    pe.wait_ge(s["x"], g.at(1))
                    need(pe, s["h"], g.at(-1), n)
                    pe.sem_inc(s["pe_passed"], 1)
                    pe.matmul(bank[4 + 3 * g.ring(2)][0:F, :], C["center"][0:F, 0:F], x[:, g.ring(4), :], start=True, stop=True) \
                        .then_inc(s["centered"], 1)

                def variance(g):
                    pe.wait_ge(s["squared"], g.at(1))
                    need(pe, s["std"], g.at())
                    pe.sem_inc(s["pe_passed"], 1)
                    pe.matmul(bank[5][0:F, :], C["mean"][0:F, 0:F], square[:, g.ring(2), :], start=True, stop=True) \
                        .then_inc(s["var"], 1)

                def turn_back(g):
                    pe.wait_ge(made_last, g.at(1))
                    need(pe, s["rows"], g.at())
                    pe.sem_inc(s["pe_passed"], 1)
                    for t in range(GT):
                        fin = pe.transpose(bank[6][:, t * F:t * F + F],
                                           hs_buf[:, g.ring(4 if last else 2), t * P:t * P + P], C["ident"][0:F, 0:F])
                    fin.then_inc(s["turned_back"], 1)
                parts = [(1, turn), (2, product)] + ([(4, variance)] if norm else []) + [(TURN_BACK, turn_back)]
                pipeline(pe, n, parts + ([(3, center)] if norm else []))

            @block.scalar
            def _(act):
                act.preload_act_table_set("natural_log_exp_and_others")

                def relu(g):
                    k = g.ring(2)
                    act.wait_ge(s["scaled"], g.at(1))
                    need(act, s["hs"], g.at(-1), n)
                    act.activation(h[:, k, :], scaled[:, k, :], ACT.Relu, bias=bias).then_inc(s["h"], 1)

                def squares(g):
                    act.wait_ge(s["centered"], g.at(1))
                    need(act, s["var"], g.at(-1), n)
                    act.activation(square[:, g.ring(2), :], bank[4 + 3 * g.ring(2)][0:F, :], ACT.Square).then_inc(s["squared"], 1)

                def deviation(g):
                    k = g.ring(2)
                    act.wait_ge(s["var"], g.at(1))
                    act.activation(std[:, k, :], bank[5][0:F, :], ACT.Ln, bias=C["eps"][0:F, 0:1]).then_inc(s["std"], 1)
                    act.wait_ge(s["std"], g.at(1))
                    need(act, s["h"], g.at(-1), n)
                    act.activation(rstd[:, k, :], std[:, k, :], ACT.Exp, scale=-0.5).then_inc(s["rstd"], 1)

                def copy_rows(g):
                    k = g.ring(2)
                    act.wait_ge(s["turned_back"], g.at(1))
                    if last:
                        need(act, s["sent"][k], g.turn(2) * (16 * GT))
                    else:
                        need(act, s["rows_stored"][k], g.turn(2) * 16)
                    act.activation(rows[:, k, :], bank[6][:, 0:GT * F], ACT.Copy).then_inc(s["rows"], 1)
                parts = ([(2, relu)] if mid else []) + ([(4, deviation)] if norm else [])
                pipeline(act, n, parts + [(TURN_BACK, copy_rows)] + ([(3, squares)] if norm else []))

            @block.vector
            def _(v):
                def finish(g):
                    k = g.ring(2)
                    v.wait_ge(s["product"], g.at(1))
                    need(v, s["h"] if mid else (s["y"] if last else s["x"]), g.at(-1), n)
                    v.tensor_tensor(scaled[:, k, :], bank[2 + k][0:F, :], factor[:, g.ring(4), :], ALU.mult) \
                        .then_inc(s["scaled"], 1)
                    if mid:
                        return
                    v.wait_ge(s["scaled"], g.at(1))
                    need(v, s["turned_back"] if last else s["centered"], g.at(-3), n)
                    if norm and first:
                        need(v, s["res"], g.at(-3), n)
                    if stage == "D":
                        need(v, s["kept_x"][g.ring(4)], g.turn(4) * 16)
                    if first:
                        v.tensor_tensor(x[:, g.ring(4), :], scaled[:, k, :], base[:, g.ring(4), :], ALU.add).then_inc(s["x"], 1)
                    elif norm:
                        v.scalar_tensor_tensor(x[:, g.ring(4), :], scaled[:, k, :], bias, base[:, g.ring(4), :],
                                               ALU.add, ALU.add).then_inc(s["x"], 1)
                    else:
                        need(v, s["x"], g.at(-1), n)
                        v.scalar_tensor_tensor(y[:, k, :], scaled[:, k, :], bias, h3in[:, g.ring(4), :],
                                               ALU.add, ALU.add).then_inc(s["y"], 1)
                        v.wait_ge(s["y"], g.at(1))
                        v.scalar_tensor_tensor(x[:, g.ring(4), :], y[:, k, :], 0.0, base[:, g.ring(4), :],
                                               ALU.max, ALU.add).then_inc(s["x"], 1)

                def sum_runs(g):
                    k = g.ring(2)
                    start = isinstance(g.at(), int) and g.at() == 0
                    v.wait_ge(s["turned"], g.at(1))
                    need(v, s["given"], g.at(1))
                    need(v, s["total"], g.at(-3), n)
                    v.tensor_tensor(part[0:F, g.ring(4), :], bank[k][0:F, :], given[:, k, :], ALU.add) \
                        .then_inc(s["part"], 1)
                    v.wait_ge(s["part"], g.at(1))
                    need(v, s["product"] if first else s["full"], g.at(-1), n)
                    need(v, s["total"], g.at())
                    v.tensor_tensor_scan(total[:, k, :], same[:, g.ring(4), :], part[:, g.ring(4), :],
                                         0.0 if start else total[:, 1 - k, W - 1:W], ALU.mult, ALU.add) \
                        .then_inc(s["total"], 1)
                    if not first:
                        v.wait_ge(s["total"], g.at(1))
                        need(v, s["product"], g.at(-1), n)
                        v.tensor_tensor(full[:, k, :], total[:, k, :], before[:, g.ring(4), :], ALU.add) \
                            .then_inc(s["full"], 1)

                def normalise(g):
                    k = g.ring(2)
                    v.wait_ge(s["rstd"], g.at(1))
                    need(v, s["hs"], g.at(-1), n)
                    if stage == "D":
                        kept_free(v, g)
                    v.scalar_tensor_tensor(h[:, k, :], bank[4 + 3 * k][0:F, :], 0.0, rstd[:, k, :], ALU.max, ALU.mult) \
                        .then_inc(s["h"], 1)
                    if first:
                        v.wait_ge(s["h"], g.at(1))
                        kept_free(v, g)
                        v.tensor_tensor(res[:, k, :], x[:, g.ring(4), :], h[:, k, :], ALU.add).then_inc(s["res"], 1)

                def scale(g):
                    k = g.ring(2)
                    v.wait_ge(s["h"], g.at(1))
                    kept_free(v, g)
                    need(v, s["turned_back"], g.at(-1), n)
                    if norm:
                        v.wait_ge(s["loaded_late"][g.ring(4)], g.turn(4) * 16 + 16)
                    v.tensor_tensor(hs[:, k, :], h[:, k, :], (nfactor if norm else factor)[:, g.ring(4), :],
                                    ALU.mult).then_inc(s["hs"], 1)

                def give(g):
                    k = g.ring(2)
                    v.wait_ge(s["loaded"][g.ring(4)], loaded(g))
                    need(v, s["part"], g.at(-1), n)
                    v.tensor_tensor(given[:, k, :], own[:, g.ring(4), :], local[:, g.ring(4), :], ALU.mult) \
                        .then_inc(s["given"], 1)
                    if first:
                        v.wait_ge(s["gathered"][k], g.turn(2) * (16 * GT) + 16 * GT)
                        need(v, s["turned"], g.at(-1), n)
                        v.tensor_tensor(
                            gs[:, k, :].rearrange("p (t f) -> p t f", f=F),
                            ring[:, k, :].rearrange("p (t f) -> p t f", f=F),
                            C["oscale"][:, bass.ds(g.at() * GT, GT)].rearrange("p (t o) -> p t o", o=1)
                            .broadcast_to([P, GT, F]), ALU.mult).then_inc(s["gs"], 1)
                parts = [(2, finish), (1, sum_runs)] + ([(4, normalise)] if norm else [])
                pipeline(v, n, parts + ([] if last else [(SCALE, scale)]) + [(0, give)])


_INS = ["x", "src", "dst", "edge_attr_32", "L0_gnn_W_msg_w", "L0_gnn_W_msg_b", "L0_gnn_W_w", "L0_gnn_W_b",
        "L0_gnn_a", "L1_gnn_fc_w", "L1_gnn_fc_b", "L2_gnn_W1", "L2_gnn_b1", "L2_gnn_W2", "L2_gnn_b2",
        "L3_gnn_W1", "L3_gnn_b1", "L3_gnn_W2", "L3_gnn_b2"]


def kernel(**inputs):
    import numpy as _np
    import concourse.bacc as _bacc
    from concourse import mybir as _mybir
    from concourse.bass_utils import run_bass_kernel_spmd as _run

    nc = _bacc.Bacc("TRN2", target_bir_lowering=False, num_devices=1)
    arrays, args = {}, {}
    for name in _INS:
        a = _np.ascontiguousarray(inputs[name])
        arrays[f"in_{name}_dram"] = a
        args[name] = nc.dram_tensor(f"in_{name}_dram", a.shape, _mybir.dt.from_np(a.dtype),
                                    kind="ExternalInput").ap()
    out = nc.dram_tensor("out_0_dram", (N, F), F32, kind="ExternalOutput").ap()
    build(nc, args, out)
    r = _run(nc, [arrays], core_ids=[0])
    return r.results[0]["out_0_dram"]
```
